# Optimizing a Trainium2 kernel written in Bass

```python
import numpy as np
import jax
import jax.numpy as jnp

def _softmax(x, axis=-1):
    return jax.nn.softmax(x, axis=axis)

def _gelu(x):
    return jax.nn.gelu(x, approximate=True)

def _silu(x):
    return jax.nn.silu(x)

def _sigmoid(x):
    return jax.nn.sigmoid(x)

def _layernorm(x, axis=-1, eps=1e-05):
    m = jnp.mean(x, axis=axis, keepdims=True)
    v = jnp.var(x, axis=axis, keepdims=True)
    return (x - m) / jnp.sqrt(v + eps)

def _scatter_add(tgt, idx, src, axis=0):
    return tgt.at[idx].add(src)

def _segment_sum(src, seg, n):
    return jax.ops.segment_sum(src, seg, n)
kernel_name = 'mk_adj_preln_d1_adj_r2_5b83a6'

def setup_inputs(seed: int=0):
    np.random.seed(seed)
    _w = jnp.asarray

    def _rec_inputs():
        import jax
        import jax.numpy as jnp
        _gk = jax.random.key(seed)
        x = 0.0001732 + 1 * jax.random.normal(jax.random.fold_in(_gk, 1), (5120, 64), jnp.float32)
        _a = jax.random.bernoulli(jax.random.fold_in(_gk, 2), 0.000390625, (5120, 5120))
        _af = _a.astype(jnp.float32)
        _af = _af * jax.random.uniform(jax.random.fold_in(_gk, 3), (5120, 5120), jnp.float32, 0.05, 0.02)
        adj = _af
        return (x, adj)
    x, adj = _rec_inputs()

    def _L0_gnn_setup():
        import jax, jax.numpy as jnp
        import numpy as np
        N_USERS = 2048
        N_ITEMS = 3072
        EMB = 64
        LN_EPS = 1e-05
        key = jax.random.key(seed)
        ks = jax.random.split(key, 10)
        N = N_USERS + N_ITEMS
        ego = jax.random.normal(ks[0], (N, EMB), jnp.float32)
        adj = (jax.random.uniform(ks[1], (N, N), jnp.float32) < 0.01).astype(jnp.float32) * 0.02
        xav = float(np.sqrt(6.0 / (EMB + EMB)))
        W_u = jax.random.uniform(ks[2], (EMB, EMB), jnp.float32, -xav, xav)
        W_i = jax.random.uniform(ks[3], (EMB, EMB), jnp.float32, -xav, xav)
        diag_u = jax.random.uniform(ks[4], (N_USERS,), jnp.float32, 0.99, 1.01)
        diag_i = jax.random.uniform(ks[5], (N_ITEMS,), jnp.float32, 0.99, 1.01)
        par_u = jax.random.uniform(ks[6], (2,), jnp.float32, 0.0, 0.99)
        par_i = jax.random.uniform(ks[7], (2,), jnp.float32, 0.0, 0.99)
        ln_gamma = jnp.ones((EMB,), jnp.float32)
        ln_beta = jnp.zeros((EMB,), jnp.float32)
        return {'ego_embeddings': ego, 'adj': adj, 'W_u': W_u, 'diag_u': diag_u, 'par_u': par_u, 'W_i': W_i, 'diag_i': diag_i, 'par_i': par_i, 'ln_gamma': ln_gamma, 'ln_beta': ln_beta}
    _L0_gnn_all = _L0_gnn_setup()
    _L0_gnn_in = {k: v for k, v in _L0_gnn_all.items() if k in ('W_u', 'diag_u', 'par_u', 'W_i', 'diag_i', 'par_i', 'ln_gamma', 'ln_beta')}
    del _L0_gnn_all
    return {'x': x, 'adj': adj, 'L0_gnn_W_u': _L0_gnn_in['W_u'], 'L0_gnn_diag_u': _L0_gnn_in['diag_u'], 'L0_gnn_par_u': _L0_gnn_in['par_u'], 'L0_gnn_W_i': _L0_gnn_in['W_i'], 'L0_gnn_diag_i': _L0_gnn_in['diag_i'], 'L0_gnn_par_i': _L0_gnn_in['par_i'], 'L0_gnn_ln_gamma': _L0_gnn_in['ln_gamma'], 'L0_gnn_ln_beta': _L0_gnn_in['ln_beta']}

def reference(x, adj, L0_gnn_W_u, L0_gnn_diag_u, L0_gnn_par_u, L0_gnn_W_i, L0_gnn_diag_i, L0_gnn_par_i, L0_gnn_ln_gamma, L0_gnn_ln_beta):
    import jax
    import jax.numpy as jnp

    def _L0_gnn_ref(ego_embeddings, adj, W_u, diag_u, par_u, W_i, diag_i, par_i, ln_gamma, ln_beta):
        import jax, jax.numpy as jnp
        import numpy as np
        N_USERS = 2048
        N_ITEMS = 3072
        EMB = 64
        LN_EPS = 1e-05
        nu = diag_u.shape[0]
        res = ego_embeddings
        ego_u = ego_embeddings[:nu]
        ego_i = ego_embeddings[nu:]
        u = par_u[0] * par_u[1] * (diag_u[:, None] * ego_u @ W_u) + ego_u
        i = par_i[0] * par_i[1] * (diag_i[:, None] * ego_i @ W_i) + ego_i
        e = jnp.concatenate([u, i], axis=0)
        h = adj @ (adj.T @ e)
        mu = jnp.mean(h, axis=-1, keepdims=True)
        var = jnp.var(h, axis=-1, keepdims=True)
        out = (h - mu) * jax.lax.rsqrt(var + LN_EPS) * ln_gamma + ln_beta + res
        return out
    h = jnp.maximum(_layernorm(x, axis=-1), 0.0)
    x = x + _L0_gnn_ref(h, adj, L0_gnn_W_u, L0_gnn_diag_u, L0_gnn_par_u, L0_gnn_W_i, L0_gnn_diag_i, L0_gnn_par_i, L0_gnn_ln_gamma, L0_gnn_ln_beta)
    return x

_drawn_inputs = setup_inputs


def setup_inputs(seed=0):
    import zlib

    import numpy as np

    out = dict(_drawn_inputs(seed))
    spreads = {'L0_gnn_ln_gamma': (1.0, 0.2), 'L0_gnn_ln_beta': (0.0, 0.1)}
    factors = {'L0_gnn_diag_u': 8.0, 'L0_gnn_W_i': 4.257, 'L0_gnn_diag_i': 8.0}
    for name, (base, spread) in spreads.items():
        noise = np.random.default_rng([zlib.crc32(name.encode()), seed]).standard_normal(out[name].shape)
        drawn = base * np.exp(spread * noise) if base else spread * noise
        out[name] = jnp.asarray(drawn.astype(out[name].dtype))
    for name, factor in factors.items():
        out[name] = (out[name] * factor).astype(out[name].dtype)
    return out
```

```python
import numpy as np
import concourse.bass as bass
from concourse import mybir
from contextlib import ExitStack

FP32 = mybir.dt.float32
ALU = mybir.AluOpType
ACT = mybir.ActivationFunctionType
AX = mybir.AxisListType

P = 128
N = 5120
D = 64
USERS = 2048
EPS = 1e-5
TILES = N // P
USER_TILES = USERS // P
ITEM_TILES = TILES - USER_TILES
CHUNK = 8
CHUNKS = TILES // CHUNK
W = 256
KB = W // P
STRIPS = N // W
PAIRS = STRIPS // 2
HALF = CHUNK // 2 * P
TURN = 16
Q = 32
QUADS = P // Q

PE_CHUNK = 0
BATCH = 2
BATCHES = (CHUNKS - 1) // BATCH
BATCH_COLS = BATCH * CHUNK * P
COPIES = [(u, a) for a in range(QUADS) for u in range(QUADS)]
POOL_COPIES, ACT_COPIES, DVE_COPIES = COPIES[0:2], COPIES[2:9], COPIES[9:16]
GROUP = 512 // P
GROUPS = CHUNK * KB // GROUP
USES = 1 + GROUPS
assert USES % 2 == 1


def gnn_kernel(nc, x, adj, w_u, diag_u, par_u, w_i, diag_i, par_i, gamma, beta, out, resid_dram):
    def rows_of(t, c):
        lo, hi = c * CHUNK, (c + 1) * CHUNK
        if hi <= USER_TILES:
            return t[0:USERS, :].rearrange("(p r) m -> p r m", r=USER_TILES)[:, lo:hi, :]
        lo, hi = lo - USER_TILES, hi - USER_TILES
        return t[USERS:N, :].rearrange("(p r) m -> p r m", r=ITEM_TILES)[:, lo:hi, :]

    adj_rows = [rows_of(adj, c) for c in range(CHUNKS)]
    x_rows = [rows_of(x, c) for c in range(CHUNKS)]
    out_rows = [rows_of(out, c) for c in range(CHUNKS)]
    resid_rows = [rows_of(resid_dram, c) for c in range(CHUNKS)]

    ctx = ExitStack()
    with ctx:
        def sb(name, shape):
            return ctx.enter_context(nc.sbuf_tensor(name, shape, FP32))

        def sem(name):
            return ctx.enter_context(nc.semaphore(name))

        a_in = sb("a_in", [P, 2 * CHUNKS, CHUNK, W])
        at_pe = sb("at_pe", [P, 2, KB, CHUNK * P])
        at_batch = sb("at_batch", [P, 2, BATCHES, KB, BATCH_COLS])
        moved = sb("moved", [P, BATCHES, KB * BATCH_COLS])
        e_sb = sb("e_sb", [P, TILES, D])
        tT_sb = sb("tT_sb", [P, W])
        t_sb = sb("t_sb", [P, KB, D])
        ident = sb("ident", [P, P])
        fold = sb("fold", [P, D])
        center = sb("center", [P, P])
        gamma_sb = sb("gamma_sb", [P, D])
        eps_sb = sb("eps_sb", [P, 1])
        zero_sb = sb("zero_sb", [P, 1])

        first = at_batch[:, 1, :, :, :].rearrange("p g k n -> p (g k n)")
        first_e = e_sb[:, :, :].rearrange("p r d -> p (r d)")
        last_ = a_in[:, 0:CHUNKS, :, :].rearrange("p s r m -> p (s r m)")

        def cut(base, at, *shape):
            n = int(np.prod(shape))
            v = base[:, at:at + n]
            if len(shape) == 2:
                v = v.rearrange("p (a b) -> p a b", b=shape[1])
            return v

        at = 0
        resid = cut(first, at, TILES, D); at += TILES * D
        h_sb = cut(first, at, TILES, D); at += TILES * D
        hT_sb = cut(first, at, 2, 512); at += 2 * 512
        sq0 = cut(first_e, 0, CHUNKS, 512)
        w2_u = cut(first, at, P); at += P
        w2_i = cut(first, at, P); at += P
        diag_sb = cut(first, at, TILES); at += TILES
        par_sb = cut(first, at, 4); at += 4
        par2_sb = cut(first, at, 2); at += 2
        beta_sb = cut(first, at, D); at += D
        sum0 = cut(first, at, TILES); at += TILES
        var0 = cut(first, at, TILES); at += TILES
        std0 = cut(first, at, TILES); at += TILES
        assert at <= BATCHES * KB * BATCH_COLS

        at = 0
        yT = cut(last_, at, CHUNKS, 512); at += CHUNKS * 512
        sq1 = cut(moved[:, 0, :], 0, CHUNKS, 512)
        y_sb = cut(last_, at, TILES, D); at += TILES * D
        var1 = cut(last_, at, CHUNKS, CHUNK); at += TILES
        std1 = cut(last_, at, CHUNKS, CHUNK); at += TILES
        resid1 = cut(last_, at, TILES, D); at += TILES * D
        assert at <= CHUNKS * CHUNK * W

        acc = ctx.enter_context(nc.psum_tensor("acc", [P, CHUNKS, 512], FP32))
        t_ps = ctx.enter_context(nc.psum_tensor("t_ps", [P, 512], FP32))
        turn = ctx.enter_context(nc.psum_tensor("turn", [P, 2, 512], FP32))

        x_landed = [sem(f"x_landed{c}") for c in range(CHUNKS)]
        small_landed = sem("small_landed")
        a_landed = [sem(f"a_landed{s}") for s in range(2 * CHUNKS)]
        consts_made = sem("consts_made")
        w2_zeroed = sem("w2_zeroed")
        pool_order = sem("pool_order")
        dve_order = sem("dve_order")
        act_order = sem("act_order")
        centered0 = sem("centered0")
        squared0 = sem("squared0")
        var0_made = sem("var0_made")
        std0_made = sem("std0_made")
        h_made = sem("h_made")
        h_transposed = sem("h_transposed")
        hT_copied = sem("hT_copied")
        hw_made = sem("hw_made")
        e_made = sem("e_made")
        resid_made = sem("resid_made")
        resid_parked = sem("resid_parked")
        resid_landed = [sem(f"resid_landed{c}") for c in range(CHUNKS)]
        projected = [[sem(f"projected{b}_{c}") for c in range(CHUNKS)] for b in range(2)]
        batch_moved = [[sem(f"batch_moved{b}_{g}") for g in range(BATCHES)] for b in range(2)]
        transposed = [[sem(f"transposed{b}_{g}") for g in range(BATCHES)] for b in range(2)]
        tT_copied = sem("tT_copied")
        turn_filled = sem("turn_filled")
        turn_emptied = sem("turn_emptied")
        applied = [sem(f"applied{b}") for b in range(2)]
        acc_final = sem("acc_final")
        yT_copied = sem("yT_copied")
        y_centered = sem("y_centered")
        squared1 = sem("squared1")
        var1_made = sem("var1_made")
        std1_made = sem("std1_made")
        y_scaled = sem("y_scaled")
        y_made = sem("y_made")
        out_stored = sem("out_stored")

        def quadrant_copy(b, g, u, a):
            slot = b * CHUNKS + 1 + g * BATCH
            src = a_in[u * Q:(u + 1) * Q, slot:slot + BATCH, :, :].rearrange(
                "p c r (k g i) -> p k (c r) g i", k=KB, g=QUADS)
            dst = moved[a * Q:(a + 1) * Q, g, :].rearrange("p (k r g i) -> p k r g i", k=KB, g=QUADS, i=Q)
            return dst[:, :, :, u, :], src[:, :, :, a, :]

        def wait_batch(engine, i, b, g, peeled):
            if not (peeled and b == 0):
                engine.wait_ge(transposed[1 - b][g], (i + b) * TURN)
            for c in range(1 + g * BATCH, 1 + (g + 1) * BATCH):
                engine.wait_ge(a_landed[b * CHUNKS + c], (i + 1) * TURN)

        with nc.Block() as block:

            @block.sync
            def _(sp):
                for c in range(CHUNKS):
                    sp.dma_start(resid[:, c * CHUNK:(c + 1) * CHUNK, :], x_rows[c]).then_inc(x_landed[c], 16)

                def load(b, c, column):
                    slot = b * CHUNKS + c
                    sp.dma_start(a_in[:, slot, :, :], adj_rows[c][:, :, bass.ds(column, W)])\
                        .then_inc(a_landed[slot], 16)

                for b in range(2):
                    for c in range(CHUNKS):
                        load(b, c, b * W)
                for c in range(CHUNKS):
                    sp.wait_ge(resid_made, c + 1)
                    sp.dma_start(resid_rows[c], resid[:, c * CHUNK:(c + 1) * CHUNK, :]).then_inc(resid_parked, 16)
                with sp.Fori(1, PAIRS) as i:
                    for b in range(2):
                        for c in range(CHUNKS):
                            if c != PE_CHUNK:
                                sp.wait_ge(batch_moved[b][(c - 1) // BATCH], i * TURN)
                            sp.wait_ge(projected[b][c], i * TURN)
                            load(b, c, (i * 2 + b) * W)
                sp.wait_ge(acc_final, 1)
                for c in range(CHUNKS):
                    sp.dma_start(resid1[:, c * CHUNK:(c + 1) * CHUNK, :], resid_rows[c]).then_inc(resid_landed[c], 16)
                for c in range(CHUNKS):
                    sp.wait_ge(y_made, c + 1)
                    sp.dma_start(out_rows[c], y_sb[:, c * CHUNK:(c + 1) * CHUNK, :]).then_inc(out_stored, 16)
                sp.wait_ge(out_stored, 16 * CHUNKS)

            @block.gpsimd
            def _(pool):
                g = nc.gpsimd
                g.memset(ident[:, :], 0.0).then_inc(pool_order, 1)
                g.memset(fold[:, :], 0.0).then_inc(pool_order, 1)
                g.memset(center[:, :], 0.0).then_inc(pool_order, 1)
                g.memset(w2_u, 0.0).then_inc(w2_zeroed, 1)
                g.memset(w2_i, 0.0).then_inc(w2_zeroed, 1)
                g.memset(eps_sb[:, :], EPS).then_inc(consts_made, 1)
                g.memset(zero_sb[:, :], 0.0).then_inc(pool_order, 1)
                pool.wait_ge(pool_order, 4)
                g.memset(center[0:D, 0:D], -1.0 / D).then_inc(pool_order, 1)
                g.memset(center[D:P, D:P], -1.0 / D).then_inc(pool_order, 1)
                pool.wait_ge(pool_order, 6)
                g.affine_select(out=ident[:, :], in_=ident[:, :], compare_op=ALU.not_equal, fill=1.0,
                                base=0, pattern=[[-1, P]], channel_multiplier=1).then_inc(consts_made, 1)
                g.affine_select(out=fold[:, :], in_=fold[:, :], compare_op=ALU.not_equal, fill=1.0,
                                base=0, pattern=[[-1, D]], channel_multiplier=1).then_inc(pool_order, 1)
                pool.wait_ge(pool_order, 7)
                g.affine_select(out=fold[:, :], in_=fold[:, :], compare_op=ALU.not_equal, fill=1.0,
                                base=-D, pattern=[[-1, D]], channel_multiplier=1).then_inc(consts_made, 1)
                g.affine_select(out=center[:, :], in_=center[:, :], compare_op=ALU.not_equal, fill=1.0 - 1.0 / D,
                                base=0, pattern=[[-1, P]], channel_multiplier=1).then_inc(consts_made, 1)

                def move_pair(i, peeled):
                    for b in range(2):
                        for g in range(BATCHES):
                            wait_batch(pool, i, b, g, peeled)
                            for n, (u, a) in enumerate(POOL_COPIES):
                                dst, src = quadrant_copy(b, g, u, a)
                                if n == 0:
                                    zero = zero_sb[u * Q:(u + 1) * Q, :].unsqueeze(2).unsqueeze(3).to_broadcast(
                                        [Q, KB, BATCH * CHUNK, Q])
                                    nc.gpsimd.tensor_tensor(dst, src, zero, ALU.subtract)\
                                        .then_inc(batch_moved[b][g], 1)
                                else:
                                    nc.gpsimd.tensor_copy(dst, src).then_inc(batch_moved[b][g], 1)

                for c in range(CHUNKS):
                    r = resid[:, c * CHUNK:(c + 1) * CHUNK, :]
                    pool.wait_ge(h_made, c + 1)
                    nc.gpsimd.tensor_tensor(r, r, h_sb[:, c * CHUNK:(c + 1) * CHUNK, :], ALU.add).then_inc(pool_order, 1)
                pool.wait_ge(small_landed, 16 * 10)
                for c in range(CHUNKS):
                    r = resid[:, c * CHUNK:(c + 1) * CHUNK, :]
                    pool.wait_ge(pool_order, 8 + c)
                    nc.gpsimd.tensor_tensor(r, r, beta_sb.unsqueeze(1).to_broadcast([P, CHUNK, D]), ALU.add)\
                        .then_inc(resid_made, 1)
                pool.wait_ge(consts_made, 4)
                pool.wait_ge(resid_made, CHUNKS)
                move_pair(0, True)
                with pool.Fori(1, PAIRS) as i:
                    move_pair(i, False)

                for g in range(BATCHES):
                    pool.wait_ge(batch_moved[1][g], PAIRS * TURN)
                for c in range(CHUNKS):
                    y = y_sb[:, c * CHUNK:(c + 1) * CHUNK, :]
                    pool.wait_ge(resid_landed[c], 16)
                    pool.wait_ge(y_scaled, c + 1)
                    nc.gpsimd.tensor_tensor(y, y, resid1[:, c * CHUNK:(c + 1) * CHUNK, :], ALU.add).then_inc(y_made, 1)

            @block.scalar
            def _(act):
                s = nc.scalar
                act.dma_start(diag_sb[:, 0:USER_TILES], diag_u.rearrange("(p r) -> p r", p=P)).then_inc(small_landed, 16)
                act.dma_start(diag_sb[:, USER_TILES:TILES], diag_i.rearrange("(p r) -> p r", p=P)).then_inc(small_landed, 16)
                act.dma_start(par_sb[:, 0:2], par_u.unsqueeze(0).to_broadcast([P, 2])).then_inc(small_landed, 16)
                act.dma_start(par_sb[:, 2:4], par_i.unsqueeze(0).to_broadcast([P, 2])).then_inc(small_landed, 16)
                act.dma_start(gamma_sb[:, :], gamma.unsqueeze(0).to_broadcast([P, D])).then_inc(small_landed, 16)
                act.dma_start(beta_sb, beta.unsqueeze(0).to_broadcast([P, D])).then_inc(small_landed, 16)
                act.wait_ge(w2_zeroed, 2)
                act.dma_start(w2_u[0:D, 0:D], w_u).then_inc(small_landed, 16)
                act.dma_start(w2_u[D:P, D:P], w_u).then_inc(small_landed, 16)
                act.dma_start(w2_i[0:D, 0:D], w_i).then_inc(small_landed, 16)
                act.dma_start(w2_i[D:P, D:P], w_i).then_inc(small_landed, 16)

                act.wait_ge(consts_made, 4)
                for c in range(CHUNKS):
                    act.wait_ge(centered0, c + 1)
                    s.activation(sq0[:, c, :], h_sb[:, c * CHUNK:(c + 1) * CHUNK, :].rearrange("p r d -> p (r d)"),
                                 ACT.Square).then_inc(squared0, 1)
                for c in range(CHUNKS):
                    act.wait_ge(var0_made, c + 1)
                    s.activation(std0[:, c * CHUNK:(c + 1) * CHUNK], var0[:, c * CHUNK:(c + 1) * CHUNK],
                                 ACT.Sqrt, scale=1.0 / D, bias=eps_sb[:, 0:1]).then_inc(std0_made, 1)
                for c in range(CHUNKS):
                    act.wait_ge(h_transposed, c + 1)
                    if c >= 2:
                        act.wait_ge(hw_made, c - 1)
                    s.copy(hT_sb[:, c % 2, :], turn[:, 0, :]).then_inc(hT_copied, 1)

                def take_t(st):
                    act.wait_ge(turn_filled, st * USES)
                    s.copy(t_sb[:, :, :].rearrange("p k d -> p (k d)"), turn[:, 0, 0:KB * D]).then_inc(turn_emptied, 1)

                def pair(i, peeled):
                    for b in range(2):
                        st = i * 2 + b
                        if not (peeled and b == 0):
                            take_t(st)
                        for n in range(GROUPS):
                            act.wait_ge(turn_filled, st * USES + 1 + n)
                            s.copy(at_pe[:, b, :, :].rearrange("p k n -> p (k n)")[:, n * 512:(n + 1) * 512],
                                   turn[:, (1 + n) % 2, :]).then_inc(turn_emptied, 1)
                        for g in range(BATCHES):
                            wait_batch(act, i, b, g, peeled)
                            for u, a in ACT_COPIES:
                                dst, src = quadrant_copy(b, g, u, a)
                                s.copy(dst, src).then_inc(batch_moved[b][g], 1)

                pair(0, True)
                with act.Fori(1, PAIRS) as i:
                    pair(i, False)
                take_t(STRIPS)

                def copy_yT(c):
                    act.wait_ge(acc_final, c + 1)
                    s.copy(yT[:, c, :], acc[:, c, :]).then_inc(yT_copied, 1)

                copy_yT(0)
                copy_yT(1)
                for c in range(CHUNKS):
                    act.wait_ge(y_centered, c + 1)
                    s.activation(sq1[:, c, :], acc[:, c, :], ACT.Square).then_inc(squared1, 1)
                    if c + 2 < CHUNKS:
                        copy_yT(c + 2)
                    act.wait_ge(var1_made, c + 1)
                    s.activation(std1[:, c, :], var1[:, c, :], ACT.Sqrt, scale=1.0 / D,
                                 bias=eps_sb[:, 0:1]).then_inc(std1_made, 1)

            @block.vector
            def _(dve):
                v = nc.vector
                done = [0]

                def ordered(ins):
                    done[0] += 1
                    ins.then_inc(dve_order, 1)
                    dve.wait_ge(dve_order, done[0])

                def tiles(t, c):
                    return t[:, c * CHUNK:(c + 1) * CHUNK, :]

                def per_tile(t, c):
                    return t[:, c * CHUNK:(c + 1) * CHUNK].unsqueeze(2).to_broadcast([P, CHUNK, D])

                for c in range(CHUNKS):
                    dve.wait_ge(x_landed[c], 16)
                    sums = sum0[:, c * CHUNK:(c + 1) * CHUNK]
                    ordered(v.reduce_sum(sums, tiles(resid, c), AX.X))
                    ordered(v.tensor_scalar(sums, sums, 1.0 / D, None, ALU.mult))
                    v.tensor_tensor(tiles(h_sb, c), tiles(resid, c), per_tile(sum0, c), ALU.subtract)\
                        .then_inc(centered0, 1)
                for c in range(CHUNKS):
                    dve.wait_ge(squared0, c + 1)
                    v.reduce_sum(var0[:, c * CHUNK:(c + 1) * CHUNK],
                                 sq0[:, c, :].rearrange("p (r d) -> p r d", d=D), AX.X).then_inc(var0_made, 1)
                dve.wait_ge(small_landed, 16 * 10)
                for j, (lo, hi) in enumerate(((0, USER_TILES), (USER_TILES, TILES))):
                    ordered(v.tensor_tensor(par2_sb[:, j:j + 1], par_sb[:, 2 * j:2 * j + 1],
                                            par_sb[:, 2 * j + 1:2 * j + 2], ALU.mult))
                    ordered(v.tensor_scalar(diag_sb[:, lo:hi], diag_sb[:, lo:hi], par2_sb[:, j:j + 1], None, ALU.mult))
                for c in range(CHUNKS):
                    dve.wait_ge(std0_made, c + 1)
                    r = std0[:, c * CHUNK:(c + 1) * CHUNK]
                    ordered(v.reciprocal(r, r))
                    v.scalar_tensor_tensor(out=tiles(h_sb, c), in0=tiles(h_sb, c), scalar=0.0,
                                           in1=per_tile(std0, c), op0=ALU.max, op1=ALU.mult).then_inc(h_made, 1)
                for c in range(CHUNKS):
                    dve.wait_ge(hw_made, c + 1)
                    ordered(v.tensor_tensor(tiles(e_sb, c), acc[:, c, :].rearrange("p (r d) -> p r d", d=D),
                                            per_tile(diag_sb, c), ALU.mult))
                    v.tensor_tensor(tiles(e_sb, c), tiles(e_sb, c), tiles(h_sb, c), ALU.add).then_inc(e_made, 1)

                def copy_batch(i, b, g, peeled=False):
                    wait_batch(dve, i, b, g, peeled)
                    for u, a in DVE_COPIES:
                        dst, src = quadrant_copy(b, g, u, a)
                        v.tensor_copy(dst, src).then_inc(batch_moved[b][g], 1)

                def transpose_batch(i, b, g):
                    dve.wait_ge(batch_moved[b][g], (i + 1) * TURN)
                    v.transpose(at_batch[:, b, g, :, :].rearrange("p k n -> p (k n)"), moved[:, g, :])\
                        .then_inc(transposed[b][g], TURN)

                def pair(i, peeled):
                    for b in range(2):
                        copy_batch(i, b, 0, peeled)
                        if peeled and b == 1:
                            dve.wait_ge(resid_parked, 16 * CHUNKS)
                        if not (peeled and b == 0):
                            transpose_batch(i + b - 1, 1 - b, 1)
                        copy_batch(i, b, 1, peeled)
                        dve.wait_ge(projected[b][CHUNKS - 1], (i + 1) * TURN)
                        v.tensor_copy(tT_sb[:, :], t_ps[:, 0:W]).then_inc(tT_copied, 1)
                        if not peeled:
                            dve.wait_ge(applied[b], i * TURN)
                        transpose_batch(i, b, 0)

                pair(0, True)
                with dve.Fori(1, PAIRS) as i:
                    pair(i, False)
                transpose_batch(PAIRS - 1, 1, 1)

                def by_half(t, c):
                    return tiles(t, c).rearrange("p (h r) d -> p r h d", h=2)

                for c in range(CHUNKS):
                    dve.wait_ge(squared1, c + 1)
                    v.reduce_sum(var1[:, c, :], sq1[:, c, :].rearrange("p (r d) -> p r d", d=D), AX.X)\
                        .then_inc(var1_made, 1)
                    dve.wait_ge(std1_made, c + 1)
                    ordered(v.reciprocal(std1[:, c, :], std1[:, c, :]))
                    rstd = std1[:, c, :].unsqueeze(2).to_broadcast([P, CHUNK, D])
                    ys = sq1[:, c, :].rearrange("p (r d) -> p r d", d=D)
                    ordered(v.tensor_tensor(ys, acc[:, c, :].rearrange("p (r d) -> p r d", d=D), rstd, ALU.mult))
                    v.tensor_tensor(by_half(y_sb, c), ys.rearrange("p (r h) d -> p r h d", h=2),
                                    gamma_sb[:, :].unsqueeze(1).unsqueeze(1).to_broadcast([P, CHUNK // 2, 2, D]),
                                    ALU.mult).then_inc(y_scaled, 1)

            @block.tensor
            def _(pe):
                t = nc.tensor
                pe.wait_ge(consts_made, 4)
                pe.wait_ge(small_landed, 16 * 10)
                for c in range(CHUNKS):
                    pe.wait_ge(h_made, c + 1)
                    if c:
                        pe.wait_ge(hT_copied, c)
                    for j in range(CHUNK // 2):
                        pairs = h_sb[:, c * CHUNK + 2 * j:c * CHUNK + 2 * j + 2, :].rearrange("p r d -> p (r d)")
                        ins = t.transpose(turn[:, 0, j * P:(j + 1) * P], pairs, ident[:, :])
                    ins.then_inc(h_transposed, 1)
                    pe.wait_ge(hT_copied, c + 1)
                    w2 = w2_u if c * CHUNK < USER_TILES else w2_i
                    for j in range(CHUNK // 2):
                        ins = t.matmul(acc[:, c, j * P:(j + 1) * P], hT_sb[:, c % 2, j * P:(j + 1) * P], w2,
                                       start=True, stop=True)
                    ins.then_inc(hw_made, 1)

                def fill_turn(st, slot, n, first_strip):
                    use = 1 + n
                    if use >= 2 and not (first_strip and use == 2):
                        pe.wait_ge(turn_emptied, st * USES + use - 2)
                    for j in range(GROUP):
                        r, k = (n * GROUP + j) % CHUNK, (n * GROUP + j) // CHUNK
                        ins = t.transpose(turn[:, use % 2, j * P:(j + 1) * P],
                                          a_in[:, slot, r, k * P:(k + 1) * P], ident[:, :])
                    ins.then_inc(turn_filled, 1)

                def project(st, i, b, first_strip=False):
                    for c in range(CHUNKS):
                        slot = b * CHUNKS + c
                        pe.wait_ge(a_landed[slot], (i + 1) * TURN)
                        if first_strip:
                            pe.wait_ge(e_made, c + 1)
                        for r in range(CHUNK):
                            if c == PE_CHUNK and r % 2 == 0:
                                fill_turn(st, slot, r // 2, first_strip)
                            o = (r % 2) * D
                            ins = t.matmul(t_ps[o:o + D, 0:W], e_sb[:, c * CHUNK + r, :], a_in[:, slot, r, :],
                                           start=(c == 0 and r < 2), stop=(c == CHUNKS - 1 and r >= CHUNK - 2))
                        ins.then_inc(projected[b][c], TURN)

                def turn_t(st):
                    pe.wait_ge(tT_copied, st + 1)
                    pe.wait_ge(turn_emptied, (st + 1) * USES - 1)
                    for k in range(KB):
                        ins = t.matmul(turn[:, 0, k * D:(k + 1) * D], tT_sb[:, k * P:(k + 1) * P], fold[:, :],
                                       start=True, stop=True)
                    ins.then_inc(turn_filled, 1)

                def apply(st, i, b, begin=False, end=False):
                    pe.wait_ge(turn_emptied, (st + 1) * USES)
                    for c in range(CHUNKS):
                        g, n = divmod(c - 1, BATCH)
                        if c != PE_CHUNK and n == 0:
                            pe.wait_ge(transposed[b][g], (i + 1) * TURN)
                        for k in range(KB):
                            for hf in range(2):
                                if c == PE_CHUNK:
                                    rows = at_pe[:, b, k, hf * HALF:(hf + 1) * HALF]
                                else:
                                    o = n * CHUNK * P + hf * HALF
                                    rows = at_batch[:, b, g, k, o:o + HALF]
                                ins = t.matmul(acc[hf * D:(hf + 1) * D, c, :], t_sb[:, k, :], rows,
                                               start=(begin and k == 0), stop=(end and k == KB - 1))
                        if end:
                            ins.then_inc(acc_final, 1)
                    if not end:
                        ins.then_inc(applied[b], TURN)

                project(0, 0, 0, first_strip=True)
                turn_t(0)
                project(1, 0, 1)
                apply(0, 0, 0, begin=True)
                with pe.Fori(1, PAIRS) as i:
                    turn_t(i * 2 - 1)
                    project(i * 2, i, 0)
                    apply(i * 2 - 1, i - 1, 1)
                    turn_t(i * 2)
                    project(i * 2 + 1, i, 1)
                    apply(i * 2, i, 0)
                turn_t(STRIPS - 1)
                apply(STRIPS - 1, PAIRS - 1, 1, end=True)

                for c in range(CHUNKS):
                    pe.wait_ge(yT_copied, c + 1)
                    for r in range(CHUNK // 2):
                        ins = t.matmul(acc[:, c, r * P:(r + 1) * P], yT[:, c, r * P:(r + 1) * P], center[:, :],
                                       start=True, stop=True)
                    ins.then_inc(y_centered, 1)


_INS = ['x', 'adj', 'L0_gnn_W_u', 'L0_gnn_diag_u', 'L0_gnn_par_u', 'L0_gnn_W_i', 'L0_gnn_diag_i', 'L0_gnn_par_i',
        'L0_gnn_ln_gamma', 'L0_gnn_ln_beta']


def kernel(**inputs):
    import numpy as _np
    import concourse.bacc as _bacc
    from concourse import mybir as _mybir
    from concourse.bass_utils import run_bass_kernel_spmd as _run

    nc = _bacc.Bacc("TRN2", target_bir_lowering=False, num_devices=1)
    arrays, args = {}, []
    for name in _INS:
        a = _np.ascontiguousarray(inputs[name])
        arrays[f"in_{name}_dram"] = a
        args.append(nc.dram_tensor(f"in_{name}_dram", a.shape, _mybir.dt.from_np(a.dtype), kind="ExternalInput").ap())
    out = nc.dram_tensor("out_0_dram", (N, D), _mybir.dt.float32, kind="ExternalOutput").ap()
    resid = nc.dram_tensor("resid_dram", (N, D), _mybir.dt.float32, kind="Internal").ap()
    gnn_kernel(nc, *args, out, resid)
    r = _run(nc, [arrays], core_ids=[0])
    return r.results[0]["out_0_dram"]
```

```python
import numpy as np
import concourse.bass as bass
from concourse import mybir
from contextlib import ExitStack

FP32 = mybir.dt.float32
ALU = mybir.AluOpType
ACT = mybir.ActivationFunctionType
AX = mybir.AxisListType

P = 128
N = 5120
D = 64
USERS = 2048
EPS = 1e-5
TILES = N // P
USER_TILES = USERS // P
ITEM_TILES = TILES - USER_TILES
CHUNK = 8
CHUNKS = TILES // CHUNK
W = 256
KB = W // P
STRIPS = N // W
PAIRS = STRIPS // 2
TURN = 16
Q = 32
QUADRANTS = P // Q

QUAD = CHUNK // 2
QUAD_ROWS = QUAD * P
BATCH = 3
BATCHES = (2 * CHUNKS - 1) // BATCH
BATCH_TILES = BATCH * QUAD
BATCH_ROWS = BATCH * QUAD_ROWS
MOVED_SLOTS = 2
assert 2 * CHUNKS == 1 + BATCHES * BATCH and 2 * BATCHES % MOVED_SLOTS == 0
TURN_AT = 2
COPIES = [(u, a) for a in range(QUADRANTS) for u in range(QUADRANTS)]
POOL_COPIES, ACT_COPIES, DVE_COPIES = COPIES[0:2], COPIES[2:10], COPIES[10:16]


def batch_tiles(g):
    return QUAD + g * BATCH_TILES, QUAD + (g + 1) * BATCH_TILES


def batch_chunks(g):
    lo, hi = batch_tiles(g)
    return range(lo // CHUNK, (hi - 1) // CHUNK + 1)


def gnn_kernel(nc, x, adj, w_u, diag_u, par_u, w_i, diag_i, par_i, gamma, beta, out, resid_dram):
    def rows_of(t, c):
        lo, hi = c * CHUNK, (c + 1) * CHUNK
        if hi <= USER_TILES:
            return t[0:USERS, :].rearrange("(p r) m -> p r m", r=USER_TILES)[:, lo:hi, :]
        lo, hi = lo - USER_TILES, hi - USER_TILES
        return t[USERS:N, :].rearrange("(p r) m -> p r m", r=ITEM_TILES)[:, lo:hi, :]

    adj_rows = [rows_of(adj, c) for c in range(CHUNKS)]
    x_rows = [rows_of(x, c) for c in range(CHUNKS)]
    out_rows = [rows_of(out, c) for c in range(CHUNKS)]
    resid_rows = [rows_of(resid_dram, c) for c in range(CHUNKS)]

    ctx = ExitStack()
    with ctx:
        def sb(name, shape):
            return ctx.enter_context(nc.sbuf_tensor(name, shape, FP32))

        def sem(name):
            return ctx.enter_context(nc.semaphore(name))

        a_in = sb("a_in", [P, 2 * CHUNKS, CHUNK, W])
        at_pe = sb("at_pe", [P, 2, KB, QUAD_ROWS])
        at_batch = sb("at_batch", [P, 2, BATCHES, KB, BATCH_ROWS])
        moved = sb("moved", [P, MOVED_SLOTS, KB * BATCH_ROWS])
        e_sb = sb("e_sb", [P, TILES, D])
        tT_sb = sb("tT_sb", [P, W])
        t_sb = sb("t_sb", [P, KB, D])
        ident = sb("ident", [P, P])
        center = sb("center", [P, P])
        gamma_sb = sb("gamma_sb", [P, D])
        eps_sb = sb("eps_sb", [P, 1])
        zero_sb = sb("zero_sb", [P, 1])
        warm = sb("warm", [P, 1])
        var1 = sb("var1", [P, CHUNKS, CHUNK])
        std1 = sb("std1", [P, CHUNKS, CHUNK])

        first = at_batch[:, 1, :, :, :].rearrange("p g k n -> p (g k n)")
        first_e = e_sb[:, :, :].rearrange("p r d -> p (r d)")
        last_ = a_in[:, 0:CHUNKS, :, :].rearrange("p s r m -> p (s r m)")

        def cut(base, at, *shape):
            n = int(np.prod(shape))
            v = base[:, at:at + n]
            if len(shape) == 2:
                v = v.rearrange("p (a b) -> p a b", b=shape[1])
            return v

        at = 0
        resid = cut(first, at, TILES, D); at += TILES * D
        h_sb = cut(first, at, TILES, D); at += TILES * D
        hd_sb = cut(first, at, TILES, D); at += TILES * D
        hT_sb = cut(first, at, 2, 512); at += 2 * 512
        sq0 = cut(first_e, 0, CHUNKS, 512)
        w2_u = cut(first, at, P); at += P
        w2_i = cut(first, at, P); at += P
        diag_sb = cut(first, at, TILES); at += TILES
        par_sb = cut(first, at, 4); at += 4
        par2_sb = cut(first, at, 2); at += 2
        beta_sb = cut(first, at, D); at += D
        sum0 = cut(first, at, TILES); at += TILES
        var0 = cut(first, at, TILES); at += TILES
        std0 = cut(first, at, TILES); at += TILES
        assert at <= BATCHES * KB * BATCH_ROWS

        at = 0
        yT = cut(last_, at, CHUNKS, 512); at += CHUNKS * 512
        sq1 = cut(last_, at, CHUNKS, 512); at += CHUNKS * 512
        y_sb = cut(last_, at, TILES, D); at += TILES * D
        resid1 = cut(last_, at, TILES, D); at += TILES * D
        assert at <= CHUNKS * CHUNK * W

        acc = ctx.enter_context(nc.psum_tensor("acc", [P, CHUNKS, 512], FP32))
        t_ps = ctx.enter_context(nc.psum_tensor("t_ps", [P, 512], FP32))
        turn = ctx.enter_context(nc.psum_tensor("turn", [P, 2, 512], FP32))

        x_landed = [sem(f"x_landed{c}") for c in range(CHUNKS)]
        diag_landed = sem("diag_landed")
        w_landed = sem("w_landed")
        affine_landed = sem("affine_landed")
        a_landed = [sem(f"a_landed{s}") for s in range(2 * CHUNKS)]
        eps_made = sem("eps_made")
        ident_made = sem("ident_made")
        center_made = sem("center_made")
        w2_zeroed = sem("w2_zeroed")
        pool_order = sem("pool_order")
        dve_order = sem("dve_order")
        centered0 = sem("centered0")
        squared0 = sem("squared0")
        var0_made = sem("var0_made")
        std0_made = sem("std0_made")
        h_made = sem("h_made")
        diag_made = sem("diag_made")
        hd_made = sem("hd_made")
        x_plus_h = sem("x_plus_h")
        h_transposed = sem("h_transposed")
        hT_copied = sem("hT_copied")
        hw_made = sem("hw_made")
        e_made = sem("e_made")
        resid_made = sem("resid_made")
        resid_parked = sem("resid_parked")
        resid_landed = [sem(f"resid_landed{c}") for c in range(CHUNKS)]
        projected = [[sem(f"projected{b}_{c}") for c in range(CHUNKS)] for b in range(2)]
        batch_moved = [[sem(f"batch_moved{b}_{g}") for g in range(BATCHES)] for b in range(2)]
        transposed = [[sem(f"transposed{b}_{g}") for g in range(BATCHES)] for b in range(2)]
        tT_copied = sem("tT_copied")
        turn_filled = sem("turn_filled")
        turn_emptied = sem("turn_emptied")
        t_turned = sem("t_turned")
        t_made = sem("t_made")
        applied = [sem(f"applied{b}") for b in range(2)]
        acc_final = sem("acc_final")
        yT_copied = sem("yT_copied")
        y_centered = sem("y_centered")
        squared1 = sem("squared1")
        var1_made = sem("var1_made")
        std1_made = sem("std1_made")
        y_scaled = sem("y_scaled")
        y_made = [sem(f"y_made{c}") for c in range(CHUNKS)]
        out_stored = sem("out_stored")

        def quadrant_copy(b, g, u, a):
            lo, hi = batch_tiles(g)
            strip = a_in[:, b * CHUNKS:(b + 1) * CHUNKS, :, :].rearrange("p c r m -> p (c r) m")
            src = strip[u * Q:(u + 1) * Q, lo:hi, :].rearrange("p r (k g i) -> p k r g i", k=KB, g=QUADRANTS)
            dst = moved[a * Q:(a + 1) * Q, moved_slot(b, g), :].rearrange("p (k r g i) -> p k r g i", k=KB,
                                                                          g=QUADRANTS, i=Q)
            return dst[:, :, :, u, :], src[:, :, :, a, :]

        def moved_slot(b, g):
            return (b * BATCHES + g) % MOVED_SLOTS

        def wait_batch(engine, i, b, g, peeled):
            if g >= MOVED_SLOTS:
                engine.wait_ge(transposed[b][g - MOVED_SLOTS], (i + 1) * TURN)
            elif not (peeled and b == 0):
                engine.wait_ge(transposed[1 - b][g + BATCHES - MOVED_SLOTS], (i + b) * TURN)
            for c in batch_chunks(g):
                engine.wait_ge(a_landed[b * CHUNKS + c], (i + 1) * TURN)

        with nc.Block() as block:

            @block.sync
            def _(sp):
                def load_x(c):
                    sp.dma_start(resid[:, c * CHUNK:(c + 1) * CHUNK, :], x_rows[c]).then_inc(x_landed[c], 16)

                load_x(0)
                sp.dma_start(diag_sb[:, 0:USER_TILES], diag_u.rearrange("(p r) -> p r", p=P)).then_inc(diag_landed, 16)
                sp.dma_start(diag_sb[:, USER_TILES:TILES], diag_i.rearrange("(p r) -> p r", p=P)).then_inc(diag_landed, 16)
                for c in range(1, CHUNKS):
                    load_x(c)

                def load(b, c, column):
                    slot = b * CHUNKS + c
                    sp.dma_start(a_in[:, slot, :, :], adj_rows[c][:, :, bass.ds(column, W)])\
                        .then_inc(a_landed[slot], 16)

                for b in range(2):
                    for c in range(CHUNKS):
                        load(b, c, b * W)
                for c in range(CHUNKS):
                    sp.wait_ge(resid_made, c + 1)
                    sp.dma_start(resid_rows[c], resid[:, c * CHUNK:(c + 1) * CHUNK, :]).then_inc(resid_parked, 16)
                with sp.Fori(1, PAIRS) as i:
                    for b in range(2):
                        for c in range(CHUNKS):
                            for g in range(BATCHES):
                                if c in batch_chunks(g):
                                    sp.wait_ge(batch_moved[b][g], i * TURN)
                            sp.wait_ge(projected[b][c if c else CHUNKS - 1], i * TURN)
                            load(b, c, (i * 2 + b) * W)
                sp.wait_ge(projected[0][CHUNKS - 1], PAIRS * TURN)
                for g in range(BATCHES):
                    sp.wait_ge(batch_moved[0][g], PAIRS * TURN)
                for c in range(CHUNKS):
                    sp.dma_start(resid1[:, c * CHUNK:(c + 1) * CHUNK, :], resid_rows[c]).then_inc(resid_landed[c], 16)
                for c in range(CHUNKS):
                    sp.wait_ge(y_made[c], 1)
                    sp.dma_start(out_rows[c], y_sb[:, c * CHUNK:(c + 1) * CHUNK, :]).then_inc(out_stored, 16)
                sp.wait_ge(out_stored, 16 * CHUNKS)

            @block.gpsimd
            def _(pool):
                g = nc.gpsimd
                g.memset(w2_u, 0.0).then_inc(w2_zeroed, 1)
                g.memset(w2_i, 0.0).then_inc(w2_zeroed, 1)
                g.memset(eps_sb[:, :], EPS).then_inc(eps_made, 1)
                g.memset(ident[:, :], 0.0).then_inc(pool_order, 1)
                g.memset(center[:, :], 0.0).then_inc(pool_order, 1)
                g.memset(zero_sb[:, :], 0.0).then_inc(pool_order, 1)
                pool.wait_ge(pool_order, 1)
                g.affine_select(out=ident[:, :], in_=ident[:, :], compare_op=ALU.not_equal, fill=1.0,
                                base=0, pattern=[[-1, P]], channel_multiplier=1).then_inc(ident_made, 1)
                pool.wait_ge(pool_order, 3)
                pool.wait_ge(ident_made, 1)
                g.memset(center[0:D, 0:D], -1.0 / D).then_inc(pool_order, 1)
                g.memset(center[D:P, D:P], -1.0 / D).then_inc(pool_order, 1)
                pool.wait_ge(pool_order, 5)
                g.affine_select(out=center[:, :], in_=center[:, :], compare_op=ALU.not_equal, fill=1.0 - 1.0 / D,
                                base=0, pattern=[[-1, P]], channel_multiplier=1).then_inc(center_made, 1)

                def move_batch(i, b, g, peeled=False):
                    wait_batch(pool, i, b, g, peeled)
                    for n, (u, a) in enumerate(POOL_COPIES):
                        dst, src = quadrant_copy(b, g, u, a)
                        if n == 0:
                            zero = zero_sb[u * Q:(u + 1) * Q, :].unsqueeze(2).unsqueeze(3).to_broadcast(
                                [Q, KB, BATCH_TILES, Q])
                            nc.gpsimd.tensor_tensor(dst, src, zero, ALU.subtract).then_inc(batch_moved[b][g], 1)
                        else:
                            nc.gpsimd.tensor_copy(dst, src).then_inc(batch_moved[b][g], 1)

                pool.wait_ge(diag_made, 2)
                for c in range(CHUNKS):
                    lo, hi = c * CHUNK, (c + 1) * CHUNK
                    pool.wait_ge(h_made, c + 1)
                    nc.gpsimd.tensor_tensor(hd_sb[:, lo:hi, :], h_sb[:, lo:hi, :],
                                            diag_sb[:, lo:hi].unsqueeze(2).to_broadcast([P, CHUNK, D]),
                                            ALU.mult).then_inc(hd_made, 1)
                pool.wait_ge(center_made, 1)
                pool.wait_ge(hd_made, CHUNKS)
                move_batch(0, 0, 0, peeled=True)
                pool.wait_ge(batch_moved[0][0], TURN)
                for c in range(CHUNKS):
                    r = resid[:, c * CHUNK:(c + 1) * CHUNK, :]
                    nc.gpsimd.tensor_tensor(r, r, h_sb[:, c * CHUNK:(c + 1) * CHUNK, :], ALU.add).then_inc(x_plus_h, 1)
                pool.wait_ge(x_plus_h, CHUNKS)
                move_batch(0, 0, 1, peeled=True)
                pool.wait_ge(affine_landed, 16 * 2)
                pool.wait_ge(batch_moved[0][1], TURN)
                for c in range(CHUNKS):
                    r = resid[:, c * CHUNK:(c + 1) * CHUNK, :]
                    nc.gpsimd.tensor_tensor(r, r, beta_sb.unsqueeze(1).to_broadcast([P, CHUNK, D]), ALU.add)\
                        .then_inc(resid_made, 1)
                pool.wait_ge(resid_made, CHUNKS)
                move_batch(0, 0, 2, peeled=True)
                for g in range(BATCHES):
                    move_batch(0, 1, g, peeled=True)
                with pool.Fori(1, PAIRS) as i:
                    for b in range(2):
                        for g in range(BATCHES):
                            move_batch(i, b, g)

                for g in range(BATCHES):
                    pool.wait_ge(batch_moved[1][g], PAIRS * TURN)
                for c in range(CHUNKS - 1):
                    y = y_sb[:, c * CHUNK:(c + 1) * CHUNK, :]
                    pool.wait_ge(resid_landed[c], 16)
                    pool.wait_ge(y_scaled, c + 1)
                    nc.gpsimd.tensor_tensor(y, y, resid1[:, c * CHUNK:(c + 1) * CHUNK, :], ALU.add)\
                        .then_inc(y_made[c], 1)

            @block.scalar
            def _(act):
                s = nc.scalar
                act.dma_start(par_sb[:, 0:2], par_u.unsqueeze(0).to_broadcast([P, 2])).then_inc(diag_landed, 16)
                act.dma_start(par_sb[:, 2:4], par_i.unsqueeze(0).to_broadcast([P, 2])).then_inc(diag_landed, 16)
                act.wait_ge(w2_zeroed, 2)
                act.dma_start(w2_u[0:D, 0:D], w_u).then_inc(w_landed, 16)
                act.dma_start(w2_u[D:P, D:P], w_u).then_inc(w_landed, 16)
                act.dma_start(w2_i[0:D, 0:D], w_i).then_inc(w_landed, 16)
                act.dma_start(w2_i[D:P, D:P], w_i).then_inc(w_landed, 16)
                act.dma_start(gamma_sb[:, :], gamma.unsqueeze(0).to_broadcast([P, D])).then_inc(affine_landed, 16)
                act.dma_start(beta_sb, beta.unsqueeze(0).to_broadcast([P, D])).then_inc(affine_landed, 16)
                act.wait_ge(eps_made, 1)
                s.activation(warm[:, :], eps_sb[:, :], ACT.Sqrt)

                def square_x(c):
                    act.wait_ge(centered0, c + 1)
                    s.activation(sq0[:, c, :], h_sb[:, c * CHUNK:(c + 1) * CHUNK, :].rearrange("p r d -> p (r d)"),
                                 ACT.Square).then_inc(squared0, 1)

                def root_x(c):
                    act.wait_ge(var0_made, c + 1)
                    s.activation(std0[:, c * CHUNK:(c + 1) * CHUNK], var0[:, c * CHUNK:(c + 1) * CHUNK],
                                 ACT.Sqrt, scale=1.0 / D, bias=eps_sb[:, 0:1]).then_inc(std0_made, 1)

                def copy_hT(c):
                    act.wait_ge(h_transposed, c + 1)
                    if c >= 2:
                        act.wait_ge(hw_made, c - 1)
                    s.copy(hT_sb[:, c % 2, :], turn[:, c % 2, :]).then_inc(hT_copied, 1)

                def copy_e(c):
                    act.wait_ge(hw_made, c + 1)
                    s.copy(e_sb[:, c * CHUNK:(c + 1) * CHUNK, :].rearrange("p r d -> p (r d)"), acc[:, c, :])\
                        .then_inc(e_made, 1)

                for n in range(CHUNKS + 3):
                    for lag, step in enumerate((square_x, root_x, copy_hT, copy_e)):
                        if 0 <= n - lag < CHUNKS:
                            step(n - lag)

                def move_batch(i, b, g, peeled):
                    wait_batch(act, i, b, g, peeled)
                    for u, a in ACT_COPIES:
                        dst, src = quadrant_copy(b, g, u, a)
                        s.copy(dst, src).then_inc(batch_moved[b][g], 1)

                def pair(i, peeled):
                    for b in range(2):
                        st = i * 2 + b
                        move_batch(i, b, 0, peeled)
                        for k in range(KB):
                            act.wait_ge(turn_filled, st * KB + k + 1)
                            s.copy(at_pe[:, b, k, :], turn[:, k, :]).then_inc(turn_emptied, 1)
                        for g in range(1, BATCHES):
                            move_batch(i, b, g, peeled)

                pair(0, True)
                with act.Fori(1, PAIRS) as i:
                    pair(i, False)

                def copy_yT(c):
                    act.wait_ge(acc_final, c + 1)
                    s.copy(yT[:, c, :], acc[:, c, :]).then_inc(yT_copied, 1)

                def square_y(c):
                    act.wait_ge(y_centered, c + 1)
                    s.activation(sq1[:, c, :], acc[:, c, :], ACT.Square).then_inc(squared1, 1)

                def root_y(c):
                    act.wait_ge(var1_made, c + 1)
                    s.activation(std1[:, c, :], var1[:, c, :], ACT.Sqrt, scale=1.0 / D,
                                 bias=eps_sb[:, 0:1]).then_inc(std1_made, 1)

                for n in range(CHUNKS + 2):
                    for lag, step in enumerate((copy_yT, square_y, root_y)):
                        if 0 <= n - lag < CHUNKS:
                            step(n - lag)

            @block.vector
            def _(dve):
                v = nc.vector
                done = [0]

                def ordered(ins):
                    done[0] += 1
                    ins.then_inc(dve_order, 1)
                    dve.wait_ge(dve_order, done[0])

                def tiles(t, c):
                    return t[:, c * CHUNK:(c + 1) * CHUNK, :]

                def per_tile(t, c):
                    return t[:, c * CHUNK:(c + 1) * CHUNK].unsqueeze(2).to_broadcast([P, CHUNK, D])

                def center_x(c):
                    dve.wait_ge(x_landed[c], 16)
                    ordered(v.reduce_sum(sum0[:, c * CHUNK:(c + 1) * CHUNK], tiles(resid, c), AX.X))
                    v.scalar_tensor_tensor(out=tiles(h_sb, c), in0=per_tile(sum0, c), scalar=-1.0 / D,
                                           in1=tiles(resid, c), op0=ALU.mult, op1=ALU.add).then_inc(centered0, 1)

                def var_x(c):
                    dve.wait_ge(squared0, c + 1)
                    v.reduce_sum(var0[:, c * CHUNK:(c + 1) * CHUNK],
                                 sq0[:, c, :].rearrange("p (r d) -> p r d", d=D), AX.X).then_inc(var0_made, 1)

                def make_h(c):
                    dve.wait_ge(std0_made, c + 1)
                    r = std0[:, c * CHUNK:(c + 1) * CHUNK]
                    ordered(v.reciprocal(r, r))
                    v.scalar_tensor_tensor(out=tiles(h_sb, c), in0=tiles(h_sb, c), scalar=0.0,
                                           in1=per_tile(std0, c), op0=ALU.max, op1=ALU.mult).then_inc(h_made, 1)

                for n in range(CHUNKS + 2):
                    for lag, step in enumerate((center_x, var_x, make_h)):
                        if 0 <= n - lag < CHUNKS:
                            step(n - lag)
                    if n == 1:
                        dve.wait_ge(diag_landed, 16 * 4)
                        for j, (lo, hi) in enumerate(((0, USER_TILES), (USER_TILES, TILES))):
                            ordered(v.tensor_tensor(par2_sb[:, j:j + 1], par_sb[:, 2 * j:2 * j + 1],
                                                    par_sb[:, 2 * j + 1:2 * j + 2], ALU.mult))
                            v.tensor_scalar(diag_sb[:, lo:hi], diag_sb[:, lo:hi], par2_sb[:, j:j + 1], None, ALU.mult)\
                                .then_inc(diag_made, 1)

                def copy_batch(i, b, g, peeled=False):
                    wait_batch(dve, i, b, g, peeled)
                    for u, a in DVE_COPIES:
                        dst, src = quadrant_copy(b, g, u, a)
                        v.tensor_copy(dst, src).then_inc(batch_moved[b][g], 1)

                def transpose_batch(i, b, g):
                    dve.wait_ge(batch_moved[b][g], (i + 1) * TURN)
                    v.transpose(at_batch[:, b, g, :, :].rearrange("p k n -> p (k n)"), moved[:, moved_slot(b, g), :])\
                        .then_inc(transposed[b][g], TURN)

                def add_halves(st):
                    dve.wait_ge(t_turned, st + 1)
                    halves = turn[:, 0, 0:KB * P].rearrange("p (k h d) -> p k d h", k=KB, h=2)
                    v.reduce_sum(t_sb[:, :, :], halves, AX.X).then_inc(t_made, 1)

                def pair(i, peeled):
                    for b in range(2):
                        after_first = not (peeled and b == 0)
                        if after_first:
                            add_halves(i * 2 + b - 1)
                        copy_batch(i, b, 0, peeled)
                        if after_first:
                            transpose_batch(i + b - 1, 1 - b, BATCHES - 1)
                        copy_batch(i, b, 1, peeled)
                        if peeled and b == 1:
                            dve.wait_ge(resid_parked, 16 * CHUNKS)
                        if not peeled:
                            dve.wait_ge(applied[b], i * TURN)
                        transpose_batch(i, b, 0)
                        dve.wait_ge(projected[b][CHUNKS - 1], (i + 1) * TURN)
                        v.tensor_copy(tT_sb[:, :], t_ps[:, 0:W]).then_inc(tT_copied, 1)
                        copy_batch(i, b, 2, peeled)
                        transpose_batch(i, b, 1)

                pair(0, True)
                with dve.Fori(1, PAIRS) as i:
                    pair(i, False)
                add_halves(STRIPS - 1)
                transpose_batch(PAIRS - 1, 1, BATCHES - 1)

                def by_half(t, c):
                    return tiles(t, c).rearrange("p (h r) d -> p r h d", h=2)

                def var_y(c):
                    dve.wait_ge(squared1, c + 1)
                    v.reduce_sum(var1[:, c, :], sq1[:, c, :].rearrange("p (r d) -> p r d", d=D), AX.X)\
                        .then_inc(var1_made, 1)

                def scale_y(c):
                    dve.wait_ge(std1_made, c + 1)
                    ordered(v.reciprocal(std1[:, c, :], std1[:, c, :]))
                    rstd = std1[:, c, :].unsqueeze(2).to_broadcast([P, CHUNK, D])
                    ys = sq1[:, c, :].rearrange("p (r d) -> p r d", d=D)
                    ordered(v.tensor_tensor(ys, acc[:, c, :].rearrange("p (r d) -> p r d", d=D), rstd, ALU.mult))
                    ins = v.tensor_tensor(by_half(y_sb, c), ys.rearrange("p (r h) d -> p r h d", h=2),
                                          gamma_sb[:, :].unsqueeze(1).unsqueeze(1).to_broadcast([P, CHUNK // 2, 2, D]),
                                          ALU.mult)
                    if c < CHUNKS - 1:
                        ins.then_inc(y_scaled, 1)
                    else:
                        ordered(ins)
                        dve.wait_ge(resid_landed[c], 16)
                        v.tensor_tensor(tiles(y_sb, c), tiles(y_sb, c), tiles(resid1, c), ALU.add)\
                            .then_inc(y_made[c], 1)

                dve.wait_ge(affine_landed, 16 * 2)
                for n in range(CHUNKS + 1):
                    for lag, step in enumerate((var_y, scale_y)):
                        if 0 <= n - lag < CHUNKS:
                            step(n - lag)

            @block.tensor
            def _(pe):
                t = nc.tensor
                pe.wait_ge(ident_made, 1)

                def turn_h(c):
                    pe.wait_ge(hd_made, c + 1)
                    if c >= 2:
                        pe.wait_ge(hT_copied, c - 1)
                    for j in range(CHUNK // 2):
                        pair = hd_sb[:, c * CHUNK + 2 * j:c * CHUNK + 2 * j + 2, :].rearrange("p r d -> p (r d)")
                        ins = t.transpose(turn[:, c % 2, j * P:(j + 1) * P], pair, ident[:, :])
                    ins.then_inc(h_transposed, 1)

                def make_e(c):
                    if c == 0:
                        pe.wait_ge(w_landed, 16 * 4)
                    t.matmul(acc[:, c, :], ident[:, :], h_sb[:, c * CHUNK:(c + 1) * CHUNK, :].rearrange(
                        "p r d -> p (r d)"), start=True, stop=False)
                    pe.wait_ge(hT_copied, c + 1)
                    w2 = w2_u if c * CHUNK < USER_TILES else w2_i
                    for j in range(CHUNK // 2):
                        ins = t.matmul(acc[:, c, j * P:(j + 1) * P], hT_sb[:, c % 2, j * P:(j + 1) * P], w2,
                                       start=False, stop=(j == CHUNK // 2 - 1))
                    ins.then_inc(hw_made, 1)

                def turn_quad(st, b, k):
                    for r in range(QUAD):
                        ins = t.transpose(turn[:, k, r * P:(r + 1) * P],
                                          a_in[:, b * CHUNKS, r, k * P:(k + 1) * P], ident[:, :])
                    ins.then_inc(turn_filled, 1)

                def project_chunk(st, i, b, c, turn_at=TURN_AT):
                    slot = b * CHUNKS + c
                    pe.wait_ge(a_landed[slot], (i + 1) * TURN)
                    for r in range(CHUNK):
                        if c == turn_at and r % 4 == 0:
                            k = r // 4
                            if turn_at == TURN_AT:
                                pe.wait_ge(turn_emptied, st * KB + k - 1)
                                if k == 0:
                                    pe.wait_ge(t_made, st)
                            turn_quad(st, b, k)
                        o = (r % 2) * D
                        ins = t.matmul(t_ps[o:o + D, 0:W], e_sb[:, c * CHUNK + r, :], a_in[:, slot, r, :],
                                       start=(c == 0 and r < 2), stop=(c == CHUNKS - 1 and r >= CHUNK - 2))
                    ins.then_inc(projected[b][c], TURN)

                def project(st, i, b):
                    for c in range(CHUNKS):
                        project_chunk(st, i, b, c)

                def turn_t(st):
                    pe.wait_ge(tT_copied, st + 1)
                    pe.wait_ge(turn_emptied, (st + 1) * KB)
                    for k in range(KB):
                        ins = t.transpose(turn[:, 0, k * P:(k + 1) * P], tT_sb[:, k * P:(k + 1) * P], ident[:, :])
                    ins.then_inc(t_turned, 1)

                def apply_chunk(i, b, c, begin=False, end=False):
                    for q in (2 * c, 2 * c + 1):
                        g, n = divmod(q - 1, BATCH)
                        if q > 0 and n == 0:
                            pe.wait_ge(transposed[b][g], (i + 1) * TURN)
                    for k in range(KB):
                        for q in (2 * c, 2 * c + 1):
                            g, n = divmod(q - 1, BATCH)
                            if q == 0:
                                rows = at_pe[:, b, k, :]
                            else:
                                rows = at_batch[:, b, g, k, n * QUAD_ROWS:(n + 1) * QUAD_ROWS]
                            o = (q % 2) * D
                            ins = t.matmul(acc[o:o + D, c, :], t_sb[:, k, :], rows,
                                           start=(begin and k == 0), stop=(end and k == KB - 1))
                    return ins

                def apply(st, i, b, begin=False):
                    pe.wait_ge(t_made, st + 1)
                    for c in range(CHUNKS):
                        ins = apply_chunk(i, b, c, begin=begin)
                    ins.then_inc(applied[b], TURN)

                for n in range(CHUNKS + 2):
                    if n < CHUNKS:
                        turn_h(n)
                    if 0 <= n - 1 < CHUNKS:
                        make_e(n - 1)
                    if n >= 2:
                        pe.wait_ge(e_made, n - 1)
                        project_chunk(0, 0, 0, n - 2, turn_at=CHUNKS - 1)
                turn_t(0)
                project(1, 0, 1)
                apply(0, 0, 0, begin=True)
                with pe.Fori(1, PAIRS) as i:
                    turn_t(i * 2 - 1)
                    project(i * 2, i, 0)
                    apply(i * 2 - 1, i - 1, 1)
                    turn_t(i * 2)
                    project(i * 2 + 1, i, 1)
                    apply(i * 2, i, 0)
                turn_t(STRIPS - 1)

                pe.wait_ge(t_made, STRIPS)
                def center_y(c):
                    pe.wait_ge(yT_copied, c + 1)
                    for r in range(CHUNK // 2):
                        ins = t.matmul(acc[:, c, r * P:(r + 1) * P], yT[:, c, r * P:(r + 1) * P], center[:, :],
                                       start=True, stop=True)
                    ins.then_inc(y_centered, 1)

                pe.wait_ge(center_made, 1)
                for n in range(CHUNKS + 1):
                    if n < CHUNKS:
                        apply_chunk(PAIRS - 1, 1, n, end=True).then_inc(acc_final, 1)
                    if n >= 1:
                        center_y(n - 1)


_INS = ['x', 'adj', 'L0_gnn_W_u', 'L0_gnn_diag_u', 'L0_gnn_par_u', 'L0_gnn_W_i', 'L0_gnn_diag_i', 'L0_gnn_par_i',
        'L0_gnn_ln_gamma', 'L0_gnn_ln_beta']


def kernel(**inputs):
    import numpy as _np
    import concourse.bacc as _bacc
    from concourse import mybir as _mybir
    from concourse.bass_utils import run_bass_kernel_spmd as _run

    nc = _bacc.Bacc("TRN2", target_bir_lowering=False, num_devices=1)
    arrays, args = {}, []
    for name in _INS:
        a = _np.ascontiguousarray(inputs[name])
        arrays[f"in_{name}_dram"] = a
        args.append(nc.dram_tensor(f"in_{name}_dram", a.shape, _mybir.dt.from_np(a.dtype), kind="ExternalInput").ap())
    out = nc.dram_tensor("out_0_dram", (N, D), _mybir.dt.float32, kind="ExternalOutput").ap()
    resid = nc.dram_tensor("resid_dram", (N, D), _mybir.dt.float32, kind="Internal").ap()
    gnn_kernel(nc, *args, out, resid)
    r = _run(nc, [arrays], core_ids=[0])
    return r.results[0]["out_0_dram"]
```

```python
import numpy as np
import concourse.bass as bass
from concourse import mybir
from contextlib import ExitStack

FP32 = mybir.dt.float32
ALU = mybir.AluOpType
ACT = mybir.ActivationFunctionType
AX = mybir.AxisListType

P = 128
N = 5120
D = 64
USERS = 2048
EPS = 1e-5
TILES = N // P
USER_TILES = USERS // P
ITEM_TILES = TILES - USER_TILES
CHUNK = 8
CHUNKS = TILES // CHUNK
W = 256
KB = W // P
STRIPS = N // W
PAIRS = STRIPS // 2
WARM_UP = 54
TURN = 16
Q = 32
QUADRANTS = P // Q

QUAD = CHUNK // 2
QUAD_ROWS = QUAD * P
BATCH = 3
BATCHES = (2 * CHUNKS - 1) // BATCH
BATCH_TILES = BATCH * QUAD
BATCH_ROWS = BATCH * QUAD_ROWS
MOVED_SLOTS = 2
assert 2 * CHUNKS == 1 + BATCHES * BATCH and 2 * BATCHES % MOVED_SLOTS == 0
POOL_GAMMA = CHUNKS - 2
TURN_AT = 3
COPIES = [(u, a) for a in range(QUADRANTS) for u in range(QUADRANTS)]
POOL_COPIES, ACT_COPIES, DVE_COPIES = COPIES[0:3], COPIES[3:11], COPIES[11:16]


def batch_tiles(g):
    return QUAD + g * BATCH_TILES, QUAD + (g + 1) * BATCH_TILES


def batch_chunks(g):
    lo, hi = batch_tiles(g)
    return range(lo // CHUNK, (hi - 1) // CHUNK + 1)


def gnn_kernel(nc, x, adj, w_u, diag_u, par_u, w_i, diag_i, par_i, gamma, beta, out):
    def rows_of(t, c):
        lo, hi = c * CHUNK, (c + 1) * CHUNK
        if hi <= USER_TILES:
            return t[0:USERS, :].rearrange("(p r) m -> p r m", r=USER_TILES)[:, lo:hi, :]
        lo, hi = lo - USER_TILES, hi - USER_TILES
        return t[USERS:N, :].rearrange("(p r) m -> p r m", r=ITEM_TILES)[:, lo:hi, :]

    adj_rows = [rows_of(adj, c) for c in range(CHUNKS)]
    x_rows = [rows_of(x, c) for c in range(CHUNKS)]
    out_rows = [rows_of(out, c) for c in range(CHUNKS)]

    ctx = ExitStack()
    with ctx:
        def sb(name, shape):
            return ctx.enter_context(nc.sbuf_tensor(name, shape, FP32))

        def sem(name):
            return ctx.enter_context(nc.semaphore(name))

        a_in = sb("a_in", [P, 2 * CHUNKS, CHUNK, W])
        at_pe = sb("at_pe", [P, 2, KB, QUAD_ROWS])
        at_batch = sb("at_batch", [P, 2, BATCHES, KB, BATCH_ROWS])
        moved = sb("moved", [P, MOVED_SLOTS, KB * BATCH_ROWS])
        resid = sb("resid", [P, TILES, D])
        e_sb = sb("e_sb", [P, TILES, D])
        tT_sb = sb("tT_sb", [P, W])
        t_sb = sb("t_sb", [P, KB, D])
        ident = sb("ident", [P, P])
        center = sb("center", [P, P])
        gamma_sb = sb("gamma_sb", [P, D])
        beta_sb = sb("beta_sb", [P, D])
        eps_sb = sb("eps_sb", [P, 1])
        zero_sb = sb("zero_sb", [P, 1])
        warm = sb("warm", [P, 1])
        var1 = sb("var1", [P, CHUNKS, CHUNK])
        std1 = sb("std1", [P, CHUNKS, CHUNK])

        first = at_batch[:, 1, :, :, :].rearrange("p g k n -> p (g k n)")
        first_e = e_sb[:, :, :].rearrange("p r d -> p (r d)")
        last_ = a_in[:, 0:CHUNKS, :, :].rearrange("p s r m -> p (s r m)")

        def cut(base, at, *shape):
            n = int(np.prod(shape))
            v = base[:, at:at + n]
            if len(shape) == 2:
                v = v.rearrange("p (a b) -> p a b", b=shape[1])
            return v

        at = 0
        h_sb = cut(first, at, TILES, D); at += TILES * D
        hd_sb = cut(first, at, TILES, D); at += TILES * D
        hT_sb = cut(first, at, 2, 512); at += 2 * 512
        sq0 = cut(first_e, 0, CHUNKS, 512)
        w2_u = cut(first, at, P); at += P
        w2_i = cut(first, at, P); at += P
        diag_sb = cut(first, at, TILES); at += TILES
        par_sb = cut(first, at, 4); at += 4
        par2_sb = cut(first, at, 2); at += 2
        sum0 = cut(first, at, TILES); at += TILES
        var0 = cut(first, at, TILES); at += TILES
        std0 = cut(first, at, TILES); at += TILES
        assert at <= BATCHES * KB * BATCH_ROWS

        at = 0
        yT = cut(last_, at, CHUNKS, 512); at += CHUNKS * 512
        sq1 = cut(last_, at, CHUNKS, 512); at += CHUNKS * 512
        y_sb = cut(last_, at, TILES, D); at += TILES * D
        assert at <= CHUNKS * CHUNK * W

        acc = ctx.enter_context(nc.psum_tensor("acc", [P, CHUNKS, 512], FP32))
        t_ps = ctx.enter_context(nc.psum_tensor("t_ps", [P, 512], FP32))
        turn = ctx.enter_context(nc.psum_tensor("turn", [P, 2, 512], FP32))

        x_landed = [sem(f"x_landed{c}") for c in range(CHUNKS)]
        diag_landed = sem("diag_landed")
        par_landed = sem("par_landed")
        w_landed = sem("w_landed")
        affine_landed = sem("affine_landed")
        a_landed = [sem(f"a_landed{s}") for s in range(2 * CHUNKS)]
        eps_made = sem("eps_made")
        ident_made = sem("ident_made")
        center_made = sem("center_made")
        w2_zeroed = sem("w2_zeroed")
        pool_order = sem("pool_order")
        dve_order = sem("dve_order")
        centered0 = sem("centered0")
        squared0 = sem("squared0")
        var0_made = sem("var0_made")
        std0_made = sem("std0_made")
        h_made = sem("h_made")
        diag_made = sem("diag_made")
        hd_made = sem("hd_made")
        x_plus_h = sem("x_plus_h")
        h_transposed = sem("h_transposed")
        hT_copied = sem("hT_copied")
        hw_made = sem("hw_made")
        e_made = sem("e_made")
        resid_made = sem("resid_made")
        projected = [[sem(f"projected{b}_{c}") for c in range(CHUNKS)] for b in range(2)]
        batch_moved = [[sem(f"batch_moved{b}_{g}") for g in range(BATCHES)] for b in range(2)]
        transposed = [[sem(f"transposed{b}_{g}") for g in range(BATCHES)] for b in range(2)]
        tT_copied = sem("tT_copied")
        turn_filled = sem("turn_filled")
        turn_emptied = sem("turn_emptied")
        t_turned = sem("t_turned")
        t_made = sem("t_made")
        applied = [sem(f"applied{b}") for b in range(2)]
        acc_final = sem("acc_final")
        yT_copied = sem("yT_copied")
        y_centered = sem("y_centered")
        squared1 = sem("squared1")
        var1_made = sem("var1_made")
        std1_made = sem("std1_made")
        y_scaled = sem("y_scaled")
        times_gamma = sem("times_gamma")
        y_made = [sem(f"y_made{c}") for c in range(CHUNKS)]
        out_stored = sem("out_stored")

        def by_half(t, c):
            return t[:, c * CHUNK:(c + 1) * CHUNK, :].rearrange("p (h r) d -> p r h d", h=2)

        def ys_gamma(c):
            return (sq1[:, c, :].rearrange("p (r h d) -> p r h d", h=2, d=D),
                    gamma_sb[:, :].unsqueeze(1).unsqueeze(1).to_broadcast([P, CHUNK // 2, 2, D]))

        def quadrant_copy(b, g, u, a):
            lo, hi = batch_tiles(g)
            strip = a_in[:, b * CHUNKS:(b + 1) * CHUNKS, :, :].rearrange("p c r m -> p (c r) m")
            src = strip[u * Q:(u + 1) * Q, lo:hi, :].rearrange("p r (k g i) -> p k r g i", k=KB, g=QUADRANTS)
            dst = moved[a * Q:(a + 1) * Q, moved_slot(b, g), :].rearrange("p (k r g i) -> p k r g i", k=KB,
                                                                          g=QUADRANTS, i=Q)
            return dst[:, :, :, u, :], src[:, :, :, a, :]

        def moved_slot(b, g):
            return (b * BATCHES + g) % MOVED_SLOTS

        def wait_batch(engine, i, b, g, peeled):
            if g >= MOVED_SLOTS:
                engine.wait_ge(transposed[b][g - MOVED_SLOTS], (i + 1) * TURN)
            elif not (peeled and b == 0):
                engine.wait_ge(transposed[1 - b][g + BATCHES - MOVED_SLOTS], (i + b) * TURN)
            for c in batch_chunks(g):
                engine.wait_ge(a_landed[b * CHUNKS + c], (i + 1) * TURN)

        with nc.Block() as block:

            @block.sync
            def _(sp):
                for c in range(CHUNKS):
                    sp.dma_start(resid[:, c * CHUNK:(c + 1) * CHUNK, :], x_rows[c]).then_inc(x_landed[c], 16)
                sp.wait_ge(w2_zeroed, 2)
                for w2, w in ((w2_u, w_u), (w2_i, w_i)):
                    sp.dma_start(w2[0:D, 0:D], w).then_inc(w_landed, 16)
                    sp.dma_start(w2[D:P, D:P], w).then_inc(w_landed, 16)

                def load(b, c, column):
                    slot = b * CHUNKS + c
                    sp.dma_start(a_in[:, slot, :, :], adj_rows[c][:, :, bass.ds(column, W)])\
                        .then_inc(a_landed[slot], 16)

                for b in range(2):
                    for c in range(CHUNKS):
                        load(b, c, b * W)
                sp.dma_start(gamma_sb[:, :], gamma.unsqueeze(0).to_broadcast([P, D])).then_inc(affine_landed, 16)
                sp.dma_start(beta_sb[:, :], beta.unsqueeze(0).to_broadcast([P, D])).then_inc(affine_landed, 16)
                with sp.Fori(1, PAIRS) as i:
                    for b in range(2):
                        for c in range(CHUNKS):
                            for g in range(BATCHES):
                                if c in batch_chunks(g):
                                    sp.wait_ge(batch_moved[b][g], i * TURN)
                            sp.wait_ge(projected[b][c if c else CHUNKS - 1], i * TURN)
                            load(b, c, (i * 2 + b) * W)
                for c in range(CHUNKS):
                    sp.wait_ge(y_made[c], 1)
                    sp.dma_start(out_rows[c], y_sb[:, c * CHUNK:(c + 1) * CHUNK, :]).then_inc(out_stored, 16)
                sp.wait_ge(out_stored, 16 * CHUNKS)

            @block.gpsimd
            def _(pool):
                gp = nc.gpsimd
                gp.memset(w2_u, 0.0).then_inc(w2_zeroed, 1)
                gp.memset(w2_i, 0.0).then_inc(w2_zeroed, 1)
                gp.memset(eps_sb[:, :], EPS).then_inc(eps_made, 1)
                pool.dma_start(par_sb[:, 0:2], par_u.unsqueeze(0).to_broadcast([P, 2])).then_inc(par_landed, 16)
                pool.dma_start(par_sb[:, 2:4], par_i.unsqueeze(0).to_broadcast([P, 2])).then_inc(par_landed, 16)
                gp.memset(ident[:, :], 0.0).then_inc(pool_order, 1)
                gp.memset(center[:, :], 0.0).then_inc(pool_order, 1)
                gp.memset(zero_sb[:, :], 0.0).then_inc(pool_order, 1)
                pool.wait_ge(pool_order, 1)
                gp.affine_select(out=ident[:, :], in_=ident[:, :], compare_op=ALU.not_equal, fill=1.0,
                                 base=0, pattern=[[-1, P]], channel_multiplier=1).then_inc(ident_made, 1)
                pool.wait_ge(pool_order, 3)
                pool.wait_ge(ident_made, 1)
                gp.memset(center[0:D, 0:D], -1.0 / D).then_inc(pool_order, 1)
                gp.memset(center[D:P, D:P], -1.0 / D).then_inc(pool_order, 1)
                pool.wait_ge(pool_order, 5)
                gp.affine_select(out=center[:, :], in_=center[:, :], compare_op=ALU.not_equal, fill=1.0 - 1.0 / D,
                                 base=0, pattern=[[-1, P]], channel_multiplier=1).then_inc(center_made, 1)

                def move_batch(i, b, g, peeled=False):
                    wait_batch(pool, i, b, g, peeled)
                    for u, a in POOL_COPIES:
                        dst, src = quadrant_copy(b, g, u, a)
                        zero = zero_sb[u * Q:(u + 1) * Q, :].unsqueeze(2).unsqueeze(3).to_broadcast(
                            [Q, KB, BATCH_TILES, Q])
                        gp.tensor_tensor(dst, src, zero, ALU.subtract).then_inc(batch_moved[b][g], 1)

                pool.wait_ge(diag_made, 2)
                for c in range(CHUNKS):
                    lo, hi = c * CHUNK, (c + 1) * CHUNK
                    pool.wait_ge(h_made, c + 1)
                    gp.tensor_tensor(hd_sb[:, lo:hi, :], h_sb[:, lo:hi, :],
                                            diag_sb[:, lo:hi].unsqueeze(2).to_broadcast([P, CHUNK, D]),
                                            ALU.mult).then_inc(hd_made, 1)
                pool.wait_ge(center_made, 1)
                pool.wait_ge(hd_made, CHUNKS)
                move_batch(0, 0, 0, peeled=True)
                move_batch(0, 0, 1, peeled=True)
                for g in range(2):
                    pool.wait_ge(batch_moved[0][g], TURN)
                for c in range(CHUNKS):
                    r = resid[:, c * CHUNK:(c + 1) * CHUNK, :]
                    gp.tensor_tensor(r, r, h_sb[:, c * CHUNK:(c + 1) * CHUNK, :], ALU.add).then_inc(x_plus_h, 1)
                pool.wait_ge(x_plus_h, CHUNKS)
                move_batch(0, 0, 2, peeled=True)
                for g in range(BATCHES):
                    move_batch(0, 1, g, peeled=True)
                with pool.Fori(1, PAIRS) as i:
                    for b in range(2):
                        for g in range(BATCHES):
                            move_batch(i, b, g)

                pool.wait_ge(affine_landed, 16 * 2)
                for g in range(BATCHES):
                    pool.wait_ge(batch_moved[1][g], PAIRS * TURN)
                for c in range(CHUNKS):
                    r = resid[:, c * CHUNK:(c + 1) * CHUNK, :]
                    gp.tensor_tensor(r, r, beta_sb[:, :].unsqueeze(1).to_broadcast([P, CHUNK, D]), ALU.add)\
                        .then_inc(resid_made, 1)
                pool.wait_ge(resid_made, CHUNKS)
                for c in range(CHUNKS - 1):
                    y = y_sb[:, c * CHUNK:(c + 1) * CHUNK, :]
                    pool.wait_ge(y_scaled, c + 1)
                    if c == POOL_GAMMA:
                        gp.tensor_tensor(by_half(y_sb, c), *ys_gamma(c), ALU.mult).then_inc(times_gamma, 1)
                        pool.wait_ge(times_gamma, 1)
                    gp.tensor_tensor(y, y, resid[:, c * CHUNK:(c + 1) * CHUNK, :], ALU.add)\
                        .then_inc(y_made[c], 1)

            @block.scalar
            def _(act):
                s = nc.scalar
                act.dma_start(diag_sb[:, 0:USER_TILES], diag_u.rearrange("(p r) -> p r", p=P)).then_inc(diag_landed, 16)
                act.dma_start(diag_sb[:, USER_TILES:TILES], diag_i.rearrange("(p r) -> p r", p=P))\
                    .then_inc(diag_landed, 16)
                act.wait_ge(eps_made, 1)
                s.activation(warm[:, :], eps_sb[:, :], ACT.Sqrt)

                def square_x(c):
                    act.wait_ge(centered0, c + 1)
                    s.activation(sq0[:, c, :], h_sb[:, c * CHUNK:(c + 1) * CHUNK, :].rearrange("p r d -> p (r d)"),
                                 ACT.Square).then_inc(squared0, 1)

                def root_x(c):
                    act.wait_ge(var0_made, c + 1)
                    s.activation(std0[:, c * CHUNK:(c + 1) * CHUNK], var0[:, c * CHUNK:(c + 1) * CHUNK],
                                 ACT.Sqrt, scale=1.0 / D, bias=eps_sb[:, 0:1]).then_inc(std0_made, 1)

                def copy_hT(c):
                    act.wait_ge(h_transposed, c + 1)
                    if c >= 2:
                        act.wait_ge(hw_made, c - 1)
                    s.copy(hT_sb[:, c % 2, :], turn[:, c % 2, :]).then_inc(hT_copied, 1)

                def move_batch(i, b, g, peeled, lo=0, hi=len(ACT_COPIES)):
                    if lo == 0:
                        wait_batch(act, i, b, g, peeled)
                    for u, a in ACT_COPIES[lo:hi]:
                        dst, src = quadrant_copy(b, g, u, a)
                        s.copy(dst, src).then_inc(batch_moved[b][g], 1)

                for n in range(CHUNKS + 3):
                    for lag, step in ((0, square_x), (1, root_x), (3, copy_hT)):
                        if 0 <= n - lag < CHUNKS:
                            step(n - lag)
                    if n in (CHUNKS, CHUNKS + 1):
                        half = len(ACT_COPIES) // 2
                        lo, hi = (half, len(ACT_COPIES)) if n > CHUNKS else (0, half)
                        move_batch(0, 0, 0, True, lo, hi)
                move_batch(0, 0, 1, True)

                def pair(i, peeled):
                    for b in range(2):
                        st = i * 2 + b
                        if not (peeled and b == 0):
                            move_batch(i, b, 0, peeled)
                        for k in range(KB):
                            act.wait_ge(turn_filled, st * KB + k + 1)
                            s.copy(at_pe[:, b, k, :], turn[:, k, :]).then_inc(turn_emptied, 1)
                        for g in range(2 if peeled and b == 0 else 1, BATCHES):
                            move_batch(i, b, g, peeled)

                pair(0, True)
                with act.Fori(1, PAIRS) as i:
                    pair(i, False)

                def copy_yT(c):
                    act.wait_ge(acc_final, c + 1)
                    s.copy(yT[:, c, :], acc[:, c, :]).then_inc(yT_copied, 1)

                def square_y(c):
                    act.wait_ge(y_centered, c + 1)
                    s.activation(sq1[:, c, :], acc[:, c, :], ACT.Square).then_inc(squared1, 1)

                def root_y(c):
                    act.wait_ge(var1_made, c + 1)
                    s.activation(std1[:, c, :], var1[:, c, :], ACT.Sqrt, scale=1.0 / D,
                                 bias=eps_sb[:, 0:1]).then_inc(std1_made, 1)

                for n in range(CHUNKS + 2):
                    for lag, step in enumerate((copy_yT, square_y, root_y)):
                        if 0 <= n - lag < CHUNKS:
                            step(n - lag)

            @block.vector
            def _(dve):
                v = nc.vector
                done = [0]

                def ordered(ins):
                    done[0] += 1
                    ins.then_inc(dve_order, 1)
                    dve.wait_ge(dve_order, done[0])

                def tiles(t, c):
                    return t[:, c * CHUNK:(c + 1) * CHUNK, :]

                def per_tile(t, c):
                    return t[:, c * CHUNK:(c + 1) * CHUNK].unsqueeze(2).to_broadcast([P, CHUNK, D])

                def center_x(c):
                    dve.wait_ge(x_landed[c], 16)
                    ordered(v.reduce_sum(sum0[:, c * CHUNK:(c + 1) * CHUNK], tiles(resid, c), AX.X))
                    v.scalar_tensor_tensor(out=tiles(h_sb, c), in0=per_tile(sum0, c), scalar=-1.0 / D,
                                           in1=tiles(resid, c), op0=ALU.mult, op1=ALU.add).then_inc(centered0, 1)

                def var_x(c):
                    dve.wait_ge(squared0, c + 1)
                    v.reduce_sum(var0[:, c * CHUNK:(c + 1) * CHUNK],
                                 sq0[:, c, :].rearrange("p (r d) -> p r d", d=D), AX.X).then_inc(var0_made, 1)

                def make_h(c):
                    dve.wait_ge(std0_made, c + 1)
                    r = std0[:, c * CHUNK:(c + 1) * CHUNK]
                    ordered(v.reciprocal(r, r))
                    v.scalar_tensor_tensor(out=tiles(h_sb, c), in0=tiles(h_sb, c), scalar=0.0,
                                           in1=per_tile(std0, c), op0=ALU.max, op1=ALU.mult).then_inc(h_made, 1)

                def make_e(c):
                    dve.wait_ge(hw_made, c + 1)
                    v.tensor_tensor(tiles(e_sb, c), acc[:, c, :].rearrange("p (r d) -> p r d", d=D), tiles(h_sb, c),
                                    ALU.add).then_inc(e_made, 1)

                def copy_batch(i, b, g, peeled=False, lo=0, hi=len(DVE_COPIES)):
                    if lo == 0:
                        wait_batch(dve, i, b, g, peeled)
                    for u, a in DVE_COPIES[lo:hi]:
                        dst, src = quadrant_copy(b, g, u, a)
                        v.tensor_copy(dst, src).then_inc(batch_moved[b][g], 1)

                for n in range(CHUNKS + 5):
                    for lag, step in ((0, center_x), (1, var_x), (2, make_h), (5, make_e)):
                        if 0 <= n - lag < CHUNKS:
                            step(n - lag)
                    if n == 2:
                        dve.wait_ge(diag_landed, 16 * 2)
                        dve.wait_ge(par_landed, 16 * 2)
                        for j, (lo, hi) in enumerate(((0, USER_TILES), (USER_TILES, TILES))):
                            ordered(v.tensor_tensor(par2_sb[:, j:j + 1], par_sb[:, 2 * j:2 * j + 1],
                                                    par_sb[:, 2 * j + 1:2 * j + 2], ALU.mult))
                            v.tensor_scalar(diag_sb[:, lo:hi], diag_sb[:, lo:hi], par2_sb[:, j:j + 1], None, ALU.mult)\
                                .then_inc(diag_made, 1)
                    if n > CHUNKS:
                        g, part = divmod(n - CHUNKS - 1, 2)
                        half = len(DVE_COPIES) // 2
                        lo, hi = (half, len(DVE_COPIES)) if part else (0, half)
                        copy_batch(0, 0, g, True, lo, hi)

                def transpose_batch(i, b, g):
                    dve.wait_ge(batch_moved[b][g], (i + 1) * TURN)
                    v.transpose(at_batch[:, b, g, :, :].rearrange("p k n -> p (k n)"), moved[:, moved_slot(b, g), :])\
                        .then_inc(transposed[b][g], TURN)

                def add_halves(st):
                    dve.wait_ge(t_turned, st + 1)
                    halves = turn[:, 0, 0:KB * P].rearrange("p (k h d) -> p k d h", k=KB, h=2)
                    v.reduce_sum(t_sb[:, :, :], halves, AX.X).then_inc(t_made, 1)

                def copy_tT(i, b):
                    dve.wait_ge(projected[b][CHUNKS - 1], (i + 1) * TURN)
                    v.tensor_copy(tT_sb[:, :], t_ps[:, 0:W]).then_inc(tT_copied, 1)

                def strip(i, b, peeled=False):
                    copy_batch(i, b, 0, peeled)
                    transpose_batch(i + b - 1, 1 - b, BATCHES - 1)
                    copy_batch(i, b, 1, peeled)
                    if peeled:
                        copy_tT(i, b)
                        dve.wait_ge(x_plus_h, CHUNKS)
                        transpose_batch(i, b, 0)
                    else:
                        dve.wait_ge(applied[b], i * TURN)
                        transpose_batch(i, b, 0)
                        copy_tT(i, b)
                    copy_batch(i, b, 2, peeled)
                    transpose_batch(i, b, 1)

                transpose_batch(0, 0, 0)
                copy_tT(0, 0)
                add_halves(0)
                copy_batch(0, 0, 2, peeled=True)
                transpose_batch(0, 0, 1)
                strip(0, 1, peeled=True)
                with dve.Fori(1, PAIRS) as i:
                    for b in range(2):
                        add_halves(i * 2 + b - 1)
                        strip(i, b)
                add_halves(STRIPS - 1)
                transpose_batch(PAIRS - 1, 1, BATCHES - 1)

                def var_y(c):
                    dve.wait_ge(squared1, c + 1)
                    v.reduce_sum(var1[:, c, :], sq1[:, c, :].rearrange("p (r d) -> p r d", d=D), AX.X)\
                        .then_inc(var1_made, 1)

                def scale_y(c):
                    dve.wait_ge(std1_made, c + 1)
                    ordered(v.reciprocal(std1[:, c, :], std1[:, c, :]))
                    rstd = std1[:, c, :].unsqueeze(2).to_broadcast([P, CHUNK, D])
                    ys = sq1[:, c, :].rearrange("p (r d) -> p r d", d=D)
                    ins = v.tensor_tensor(ys, acc[:, c, :].rearrange("p (r d) -> p r d", d=D), rstd, ALU.mult)
                    if c != POOL_GAMMA:
                        ordered(ins)
                        ins = v.tensor_tensor(by_half(y_sb, c), *ys_gamma(c), ALU.mult)
                    if c < CHUNKS - 1:
                        ins.then_inc(y_scaled, 1)
                    else:
                        ordered(ins)
                        dve.wait_ge(resid_made, c + 1)
                        v.tensor_tensor(tiles(y_sb, c), tiles(y_sb, c), tiles(resid, c), ALU.add)\
                            .then_inc(y_made[c], 1)

                dve.wait_ge(affine_landed, 16 * 2)
                for n in range(CHUNKS + 1):
                    for lag, step in enumerate((var_y, scale_y)):
                        if 0 <= n - lag < CHUNKS:
                            step(n - lag)

            @block.tensor
            def _(pe):
                t = nc.tensor
                pe.wait_ge(ident_made, 1)
                for n in range(WARM_UP):
                    t.transpose(t_ps[:, 0:P], ident[:, :], ident[:, :])

                def turn_h(c):
                    pe.wait_ge(hd_made, c + 1)
                    if c >= 2:
                        pe.wait_ge(hT_copied, c - 1)
                    for j in range(CHUNK // 2):
                        pair = hd_sb[:, c * CHUNK + 2 * j:c * CHUNK + 2 * j + 2, :].rearrange("p r d -> p (r d)")
                        ins = t.transpose(turn[:, c % 2, j * P:(j + 1) * P], pair, ident[:, :])
                    ins.then_inc(h_transposed, 1)

                def times_w(c):
                    if c == 0:
                        pe.wait_ge(w_landed, 16 * 4)
                    pe.wait_ge(hT_copied, c + 1)
                    w2 = w2_u if c * CHUNK < USER_TILES else w2_i
                    for j in range(CHUNK // 2):
                        ins = t.matmul(acc[:, c, j * P:(j + 1) * P], hT_sb[:, c % 2, j * P:(j + 1) * P], w2,
                                       start=True, stop=True)
                    ins.then_inc(hw_made, 1)

                def turn_quad(st, b, k):
                    for r in range(QUAD):
                        ins = t.transpose(turn[:, k, r * P:(r + 1) * P],
                                          a_in[:, b * CHUNKS, r, k * P:(k + 1) * P], ident[:, :])
                    ins.then_inc(turn_filled, 1)

                def project_chunk(st, i, b, c, turn_at=TURN_AT):
                    slot = b * CHUNKS + c
                    pe.wait_ge(a_landed[slot], (i + 1) * TURN)
                    for r in range(CHUNK):
                        if c == turn_at and r % 4 == 0:
                            k = r // 4
                            if turn_at == TURN_AT:
                                pe.wait_ge(turn_emptied, st * KB + k - 1)
                                if k == 0:
                                    pe.wait_ge(t_made, st)
                            turn_quad(st, b, k)
                        o = (r % 2) * D
                        ins = t.matmul(t_ps[o:o + D, 0:W], e_sb[:, c * CHUNK + r, :], a_in[:, slot, r, :],
                                       start=(c == 0 and r < 2), stop=(c == CHUNKS - 1 and r >= CHUNK - 2))
                    ins.then_inc(projected[b][c], TURN)

                def project(st, i, b):
                    for c in range(CHUNKS):
                        project_chunk(st, i, b, c)

                def turn_t(st):
                    pe.wait_ge(tT_copied, st + 1)
                    pe.wait_ge(turn_emptied, (st + 1) * KB)
                    for k in range(KB):
                        ins = t.transpose(turn[:, 0, k * P:(k + 1) * P], tT_sb[:, k * P:(k + 1) * P], ident[:, :])
                    ins.then_inc(t_turned, 1)

                def apply_chunk(i, b, c, begin=False, end=False):
                    for q in (2 * c, 2 * c + 1):
                        g, n = divmod(q - 1, BATCH)
                        if q > 0 and n == 0:
                            pe.wait_ge(transposed[b][g], (i + 1) * TURN)
                    for k in range(KB):
                        for q in (2 * c, 2 * c + 1):
                            g, n = divmod(q - 1, BATCH)
                            if q == 0:
                                rows = at_pe[:, b, k, :]
                            else:
                                rows = at_batch[:, b, g, k, n * QUAD_ROWS:(n + 1) * QUAD_ROWS]
                            o = (q % 2) * D
                            ins = t.matmul(acc[o:o + D, c, :], t_sb[:, k, :], rows,
                                           start=(begin and k == 0), stop=(end and k == KB - 1))
                    return ins

                def apply(st, i, b, begin=False):
                    pe.wait_ge(t_made, st + 1)
                    for c in range(CHUNKS):
                        ins = apply_chunk(i, b, c, begin=begin)
                    ins.then_inc(applied[b], TURN)

                for n in range(CHUNKS + 2):
                    if n < CHUNKS:
                        turn_h(n)
                    if 0 <= n - 1 < CHUNKS:
                        times_w(n - 1)
                    if n >= 2:
                        pe.wait_ge(e_made, n - 1)
                        project_chunk(0, 0, 0, n - 2, turn_at=CHUNKS - 1)
                turn_t(0)
                project(1, 0, 1)
                apply(0, 0, 0, begin=True)
                with pe.Fori(1, PAIRS) as i:
                    turn_t(i * 2 - 1)
                    project(i * 2, i, 0)
                    apply(i * 2 - 1, i - 1, 1)
                    turn_t(i * 2)
                    project(i * 2 + 1, i, 1)
                    apply(i * 2, i, 0)
                turn_t(STRIPS - 1)

                def center_y(c):
                    pe.wait_ge(yT_copied, c + 1)
                    for r in range(CHUNK // 2):
                        ins = t.matmul(acc[:, c, r * P:(r + 1) * P], yT[:, c, r * P:(r + 1) * P], center[:, :],
                                       start=True, stop=True)
                    ins.then_inc(y_centered, 1)

                pe.wait_ge(t_made, STRIPS)
                pe.wait_ge(center_made, 1)
                for n in range(CHUNKS + 1):
                    if n < CHUNKS:
                        apply_chunk(PAIRS - 1, 1, n, end=True).then_inc(acc_final, 1)
                    if n >= 1:
                        center_y(n - 1)


_INS = ['x', 'adj', 'L0_gnn_W_u', 'L0_gnn_diag_u', 'L0_gnn_par_u', 'L0_gnn_W_i', 'L0_gnn_diag_i', 'L0_gnn_par_i',
        'L0_gnn_ln_gamma', 'L0_gnn_ln_beta']


def kernel(**inputs):
    import numpy as _np
    import concourse.bacc as _bacc
    from concourse import mybir as _mybir
    from concourse.bass_utils import run_bass_kernel_spmd as _run

    nc = _bacc.Bacc("TRN2", target_bir_lowering=False, num_devices=1)
    arrays, args = {}, []
    for name in _INS:
        a = _np.ascontiguousarray(inputs[name])
        arrays[f"in_{name}_dram"] = a
        args.append(nc.dram_tensor(f"in_{name}_dram", a.shape, _mybir.dt.from_np(a.dtype), kind="ExternalInput").ap())
    out = nc.dram_tensor("out_0_dram", (N, D), _mybir.dt.float32, kind="ExternalOutput").ap()
    gnn_kernel(nc, *args, out)
    r = _run(nc, [arrays], core_ids=[0])
    return r.results[0]["out_0_dram"]
```
